# Optimizing a Trainium2 kernel written in Bass

```python
import numpy as np
import jax
import jax.numpy as jnp

def _softmax(x, axis=-1):
    return jax.nn.softmax(x, axis=axis)

def _gelu(x):
    return jax.nn.gelu(x, approximate=True)

def _silu(x):
    return jax.nn.silu(x)

def _sigmoid(x):
    return jax.nn.sigmoid(x)

def _layernorm(x, axis=-1, eps=1e-05):
    m = jnp.mean(x, axis=axis, keepdims=True)
    v = jnp.var(x, axis=axis, keepdims=True)
    return (x - m) / jnp.sqrt(v + eps)

def _scatter_add(tgt, idx, src, axis=0):
    return tgt.at[idx].add(src)

def _segment_sum(src, seg, n):
    return jax.ops.segment_sum(src, seg, n)
kernel_name = 'mk_adj_preln_d1_adj_r2_99bdff'

def setup_inputs(seed: int=0):
    np.random.seed(seed)
    _w = jnp.asarray

    def _rec_inputs():
        import jax
        import jax.numpy as jnp
        _gk = jax.random.key(seed)
        x = 7.22e-05 + 1 * jax.random.normal(jax.random.fold_in(_gk, 1), (16, 512, 512), jnp.float32)
        _a = jax.random.bernoulli(jax.random.fold_in(_gk, 2), 0.00390625, (16, 512, 512))
        _a = jnp.logical_or(_a, jnp.swapaxes(_a, -1, -2))
        _a = jnp.logical_or(_a, jnp.eye(512, dtype=bool))
        adj = _a.astype(jnp.int32)
        return (x, adj)
    x, adj = _rec_inputs()

    def _L0_gnn_setup():
        import jax, jax.numpy as jnp
        import numpy as np
        import math
        D_MODEL = 512
        N_HEADS = 16
        D_HEAD = D_MODEL // N_HEADS
        B, S = (4, 1024)
        key = jax.random.key(seed)
        ks = jax.random.split(key, 10)
        x = jax.random.normal(ks[0], (B, S, D_MODEL), dtype=jnp.float32)
        mask = jax.random.randint(ks[1], (B, S, S), 0, 2, dtype=jnp.int32)
        eye = jnp.eye(S, dtype=jnp.int32)[None]
        mask = jnp.maximum(mask, eye)
        std = 1.0 / math.sqrt(D_MODEL)
        Wq = jax.random.normal(ks[2], (D_MODEL, D_MODEL), dtype=jnp.float32) * std
        Wk = jax.random.normal(ks[3], (D_MODEL, D_MODEL), dtype=jnp.float32) * std
        Wv = jax.random.normal(ks[4], (D_MODEL, D_MODEL), dtype=jnp.float32) * std
        Wo = jax.random.normal(ks[5], (D_MODEL, D_MODEL), dtype=jnp.float32) * std
        bq = jnp.zeros((D_MODEL,), dtype=jnp.float32)
        bk = jnp.zeros((D_MODEL,), dtype=jnp.float32)
        bv = jnp.zeros((D_MODEL,), dtype=jnp.float32)
        bo = jnp.zeros((D_MODEL,), dtype=jnp.float32)
        return {'x': x, 'mask': mask, 'Wq': Wq, 'bq': bq, 'Wk': Wk, 'bk': bk, 'Wv': Wv, 'bv': bv, 'Wo': Wo, 'bo': bo}
    _L0_gnn_all = _L0_gnn_setup()
    _L0_gnn_in = {k: v for k, v in _L0_gnn_all.items() if k in ('Wq', 'bq', 'Wk', 'bk', 'Wv', 'bv', 'Wo', 'bo')}
    del _L0_gnn_all
    return {'x': x, 'adj': adj, 'L0_gnn_Wq': _L0_gnn_in['Wq'], 'L0_gnn_bq': _L0_gnn_in['bq'], 'L0_gnn_Wk': _L0_gnn_in['Wk'], 'L0_gnn_bk': _L0_gnn_in['bk'], 'L0_gnn_Wv': _L0_gnn_in['Wv'], 'L0_gnn_bv': _L0_gnn_in['bv'], 'L0_gnn_Wo': _L0_gnn_in['Wo'], 'L0_gnn_bo': _L0_gnn_in['bo']}

def reference(x, adj, L0_gnn_Wq, L0_gnn_bq, L0_gnn_Wk, L0_gnn_bk, L0_gnn_Wv, L0_gnn_bv, L0_gnn_Wo, L0_gnn_bo):
    import jax
    import jax.numpy as jnp

    def _L0_gnn_ref(x, mask, Wq, bq, Wk, bk, Wv, bv, Wo, bo):
        import jax, jax.numpy as jnp
        import numpy as np
        import math
        D_MODEL = 512
        N_HEADS = 16
        D_HEAD = D_MODEL // N_HEADS
        B, S = (4, 1024)
        b, s, _ = x.shape
        scale = 1.0 / math.sqrt(D_HEAD)

        def heads(t):
            return t.reshape(b, s, N_HEADS, D_HEAD).transpose(0, 2, 1, 3)
        q = heads(x @ Wq + bq)
        k = heads(x @ Wk + bk)
        v = heads(x @ Wv + bv)
        scores = jnp.einsum('bhqd,bhkd->bhqk', q, k) * scale
        scores = jnp.where(mask[:, None] == 0, -jnp.inf, scores)
        attn = jax.nn.softmax(scores, axis=-1)
        out = jnp.einsum('bhqk,bhkd->bhqd', attn, v)
        out = out.transpose(0, 2, 1, 3).reshape(b, s, D_MODEL)
        return out @ Wo + bo
    h = jnp.maximum(_layernorm(x, axis=-1), 0.0)
    x = x + _L0_gnn_ref(h, adj, L0_gnn_Wq, L0_gnn_bq, L0_gnn_Wk, L0_gnn_bk, L0_gnn_Wv, L0_gnn_bv, L0_gnn_Wo, L0_gnn_bo)
    return x

_drawn_inputs = setup_inputs


def setup_inputs(seed=0):
    import zlib

    import numpy as np

    out = dict(_drawn_inputs(seed))
    spreads = {'L0_gnn_bq': (0.0, 0.645),
     'L0_gnn_bk': (0.0, 0.8),
     'L0_gnn_bv': (0.0, 0.1),
     'L0_gnn_bo': (0.0, 0.1)}
    factors = {}
    for name, (base, spread) in spreads.items():
        noise = np.random.default_rng([zlib.crc32(name.encode()), seed]).standard_normal(out[name].shape)
        drawn = base * np.exp(spread * noise) if base else spread * noise
        out[name] = jnp.asarray(drawn.astype(out[name].dtype))
    for name, factor in factors.items():
        out[name] = (out[name] * factor).astype(out[name].dtype)
    return out
```

```python
from contextlib import ExitStack

import concourse.bass as bass
from concourse import mybir

ALU = mybir.AluOpType
ACT = mybir.ActivationFunctionType
F32 = mybir.dt.float32
F32R = mybir.dt.float32r
BF16 = mybir.dt.bfloat16
I32 = mybir.dt.int32

P = 128
HEADS = 16
GROUP = 4
NT = 4
SLOTS = 64
S1_AT, S2_AT = 40, 60
MASKED = -1.0e30
LN_EPS = 1e-5
STACK = 96
P_RING = 8

TILES = ([("o", t) for t in range(4)]
         + [("q", 0), ("k", 0), ("q", 1), ("k", 1), ("v", 0), ("v", 1), ("q", 2), ("k", 2),
            ("v", 2), ("v", 3), ("q", 3), ("k", 3)])
QKV_TILES = [x for x in TILES if x[0] != "o"]
QK_ORDER = [x for x in TILES if x[0] in "qk"]
TURNS = {1: [("h", 0, 0)], 5: [("h", 1, 0)], 9: [("c", 1, -1)], 11: [("h", 2, 0)], 14: [("h", 3, 0)],
         25: [("c", 2, -1)], 41: [("c", 3, -1)], 50: [("m", 0, 0)], 54: [("m", 1, 0)],
         57: [("c", 0, 0)], 58: [("m", 2, 0)], 62: [("m", 3, 0)]}
TURN_LIST = [x for u in sorted(TURNS) for x in TURNS[u]]
O_EVAC = {16: 0, 32: 1, 48: 2, 63: 3}
C_AT = {9: (1, -1), 25: (2, -1), 41: (3, -1), 57: (0, 0)}


def attention_block(nc, x, adj, Wq, bq, Wk, bk, Wv, bv, Wo, bo, out):
    B, S, D = x.shape
    DH = D // HEADS
    SCALE = float(DH) ** -0.5
    assert S == NT * P and D == NT * P and DH * GROUP == P
    LOOP_FROM, LOOP_TO = 2, B - 2
    assert (LOOP_TO - LOOP_FROM) % 2 == 0

    x_rows = x.rearrange("b (t p) d -> (b t) p d", p=P)
    adj_rows = adj.rearrange("b (t p) d -> (b t) p d", p=P)
    out_rows = out.rearrange("b (t p) d -> (b t) p d", p=P)

    with ExitStack() as ctx:
        def sb(name, shape, dt):
            return ctx.enter_context(nc.sbuf_tensor(name, shape, dt))

        def sem(name):
            return ctx.enter_context(nc.semaphore(name))

        w_hi = {n: sb(f"w{n}_hi", [P, NT, D], F32R) for n in "qkvo"}
        w_lo = {n: sb(f"w{n}_lo", [P, NT, D], F32R) for n in "qkvo"}
        hT_hi = sb("hT_hi", [P, NT, S], F32R)
        hT_lo = sb("hT_lo", [P, NT, S], F32R)
        q_stack = sb("q_stack", [STACK + 2, NT, GROUP, S], F32R)
        k_stack = sb("k_stack", [STACK + 2, NT, GROUP, S], F32R)
        v_sb = sb("v_sb", [P, 2, NT, D], F32)
        oT_hi = sb("oT_hi", [P, NT, S], F32R)
        oT_lo = sb("oT_lo", [P, NT, S], F32R)
        x_tile = sb("x_tile", [P, 2, D], F32)
        adj_tile = sb("adj_tile", [P, 2, S], I32)
        bias_q = sb("bias_q", [P, NT, S], BF16)
        bias_k = sb("bias_k", [P, NT, S], BF16)
        probs = sb("probs", [P, P_RING, S], F32)
        part_hi = sb("part_hi", [P, S], F32R)
        part_lo = sb("part_lo", [P, S], F32R)
        y_tile = sb("y_tile", [P, 2, D], F32)
        bq_col = sb("bq_col", [P, NT], F32)
        bk_col = sb("bk_col", [P, NT], F32)
        bv_row = sb("bv_row", [P, D], F32)
        bo_row = sb("bo_row", [P, D], F32)
        ident = sb("ident", [P, P], F32)
        ident_b = sb("ident_b", [P, P], BF16)
        minus_half = sb("minus_half", [P, 1], F32)
        stats = sb("stats", [P, 6], F32)
        mean_var = sb("mean_var", [P, 2, 2], F32)
        var_eps = sb("var_eps", [P, 2, 1], F32)
        rstd = sb("rstd", [P, 2, 1], F32)
        neg_max = sb("neg_max", [P, 2, 16], F32)
        exp_sum = sb("exp_sum", [P, 2, 16], F32)
        ln_sum = sb("ln_sum", [P, 16], F32)
        c_all = sb("c_all", [P, 16], F32)
        c_parts = sb("c_parts", [P, 2, 16], F32R)
        c_rows = sb("c_rows", [32, P], F32R)

        ps1 = ctx.enter_context(nc.psum_tensor("ps1", [P, 2, S], F32))
        ps2 = ctx.enter_context(nc.psum_tensor("ps2", [P, 2, S], F32))
        psP = ctx.enter_context(nc.psum_tensor("psP", [P, 2, S], F32))
        psO = ctx.enter_context(nc.psum_tensor("psO", [P, S], F32))
        psT = ctx.enter_context(nc.psum_tensor("psT", [P, S], F32))

        w_in = {n: sem(f"w{n}_in") for n in "qkvo"}
        small_in = sem("small_in")
        w_hi_done, w_lo_done = sem("w_hi_done"), sem("w_lo_done")
        ident_done = sem("ident_done")
        x_in = [sem("x_in0"), sem("x_in1")]
        adj_in = [sem("adj_in0"), sem("adj_in1")]
        y_in = [sem("y_in0"), sem("y_in1")]
        y_out = [sem("y_out0"), sem("y_out1")]
        stack_in = {"q": sem("q_stack_in"), "k": sem("k_stack_in")}
        c_in = sem("c_in")
        stats_done, aggr_done = sem("stats_done"), sem("aggr_done")
        var_done, rstd_done, norm_done = sem("var_done"), sem("rstd_done"), sem("norm_done")
        h_turned, h_hi_done, h_lo_done = sem("h_turned"), sem("h_hi_done"), sem("h_lo_done")
        bias_done = sem("bias_done")
        m_turned, m_done = sem("m_turned"), sem("m_done")
        qkv_done, out_done = sem("qkv_done"), sem("out_done")
        qk_hi_done, qk_lo_done = sem("qk_hi_done"), sem("qk_lo_done")
        v_done = sem("v_done")
        scores1, masked_max, exp1_done = sem("scores1"), sem("masked_max"), sem("exp1_done")
        ln_done, c_sum_done, c_hi_done, c_lo_done = sem("ln_done"), sem("c_sum_done"), sem("c_hi_done"), sem("c_lo_done")
        c_turned, c_rows_done = sem("c_turned"), sem("c_rows_done")
        scores2, exp2_done = sem("scores2"), sem("exp2_done")
        pv_done, o_hi_done, o_lo_done = sem("pv_done"), sem("o_hi_done"), sem("o_lo_done")
        y_plus_bo, y_done = sem("y_plus_bo"), sem("y_done")

        def known(b):
            return isinstance(b, int)

        def have(b):
            return not known(b) or 0 <= b < B

        def due(count):
            return max(count, 0) if known(count) else count

        class Counter:
            def __init__(self, eng, name, step=1):
                self.eng, self.reg, self.step = eng, eng.alloc_register(name), step

            def start(self, value):
                self.eng.reg_mov(self.reg, value)

            def advance(self):
                self.eng.reg_add(self.reg, self.reg, self.step)

        def pass1(k, u):
            return (k, u - S1_AT) if u >= S1_AT else (k - 1, u + SLOTS - S1_AT)

        def pass2(k, u):
            return (k, u - S2_AT) if u >= S2_AT else (k - 1, u + SLOTS - S2_AT)

        def blocks(eng, block, first=-1, counters=()):
            for k in range(first, LOOP_FROM):
                block(k, k % 2)
            for counter, value in counters:
                counter.start(value)
            with eng.Fori(LOOP_FROM, LOOP_TO, 2) as k:
                block(k, 0)
                block(k + 1, 1)
            for k in range(LOOP_TO, B + 2):
                block(k, k % 2)

        block = ctx.enter_context(nc.Block())

        @block.sync
        def _(sp):
            next_part = Counter(sp, "next_part")
            def load_x(b, t):
                if have(b):
                    row = 4 * b + t
                    sp.wait_ge(h_turned, due(4 * b + t - 1))
                    sp.dma_start(x_tile[:, t % 2, :], x_rows[bass.ds(row, 1)].rearrange("a p d -> (a p) d")
                                 ).then_inc(x_in[t % 2], 16)

            def load_adj(b, t):
                if have(b):
                    row = 4 * b + t
                    sp.wait_ge(bias_done, due(4 * b + t - 1))
                    sp.dma_start(adj_tile[:, t % 2, :], adj_rows[bass.ds(row, 1)].rearrange("a p d -> (a p) d")
                                 ).then_inc(adj_in[t % 2], 16)

            def load_y(b, t):
                if have(b):
                    row = 4 * b + t
                    sp.wait_ge(y_out[t % 2], due(16 * (2 * b + t // 2)))
                    sp.dma_start(y_tile[:, t % 2, :], x_rows[bass.ds(row, 1)].rearrange("a p d -> (a p) d")
                                 ).then_inc(y_in[t % 2], 16)

            def store_y(b, t):
                if have(b):
                    row = 4 * b + t
                    sp.wait_ge(y_done, due(4 * b + t + 1))
                    sp.dma_start(out_rows[bass.ds(row, 1)].rearrange("a p d -> (a p) d"), y_tile[:, t % 2, :]
                                 ).then_inc(y_out[t % 2], 16)

            def load_stack(b, i):
                if not have(b):
                    return
                kind, g = QK_ORDER[i]
                stack = q_stack if kind == "q" else k_stack
                lo_row = 64 if kind == "q" else 32
                sp.wait_ge(scores2, due(64 * (b - 1) + 16 * (g + 1)))
                sp.wait_ge(qk_hi_done, due(8 * b + i + 1) if known(b) else next_part.reg)
                for row in (r for r in (0, 32, 64) if r != lo_row):
                    for j in range(GROUP):
                        sp.dma_start(stack[row:row + 32, g, j, :].bitcast(F32), part_hi[32 * j:32 * j + 32, :].bitcast(F32)
                                     ).then_inc(stack_in[kind], 16)
                sp.wait_ge(qk_lo_done, due(8 * b + i + 1) if known(b) else next_part.reg)
                for j in range(GROUP):
                    sp.dma_start(stack[lo_row:lo_row + 32, g, j, :].bitcast(F32), part_lo[32 * j:32 * j + 32, :].bitcast(F32)
                                 ).then_inc(stack_in[kind], 16)
                if not known(b):
                    next_part.advance()

            def load_c(b, g):
                if have(b):
                    sp.wait_ge(c_rows_done, due(4 * b + g + 1))
                    for part in range(2):
                        sp.dma_start(q_stack[STACK + part:STACK + part + 1, g, :, :].rearrange("a j (t q) -> a (j t) q", q=P).bitcast(F32),
                                     c_rows[16 * part:16 * part + 16, :].bitcast(F32)).then_inc(c_in, 16)

            def step(k, parity):
                for u in range(SLOTS):
                    if u == 2: load_x(k, 2)
                    if u == 6: load_x(k, 3)
                    if u == 16: load_x(k + 1, 0)
                    if u == 18: load_x(k + 1, 1)
                    if u in (20, 22, 32, 36): load_adj(k, (20, 22, 32, 36).index(u))
                    if u < 20 and u % 4 == 1 and u >= 5: store_y(k - 2, (u - 5) // 4)
                    if u in (7, 11): load_y(k - 2, (u + 1) // 4)
                    if u in (44, 46): load_y(k - 1, (u - 44) // 2)
                    if u % 4 == 1:
                        T, b = (u // 4 - 1, k) if u >= 4 else (15, k - 1)
                        if TILES[T][0] in "qk":
                            load_stack(b, QK_ORDER.index(TILES[T]))
                    if u - 1 in C_AT:
                        g, rel = C_AT[u - 1]
                        load_c(k + rel, g)

            step(-1, 1)
            for n, w in (("q", Wq), ("k", Wk), ("v", Wv), ("o", Wo)):
                at = 4 * ("qkvo".index(n) % 2)
                if n in "vo":
                    sp.wait_ge(w_lo_done, "qkvo".index(n) - 1)
                sp.dma_start(probs[:, at:at + 4, :], w.rearrange("(t p) d -> p t d", p=P)).then_inc(w_in[n], 16)
                if n == "k":
                    with nc.allow_non_contiguous_dma(reason="two bias vectors, once"):
                        sp.dma_start(bq_col[:], bq.rearrange("(t p) -> p t", p=P)).then_inc(small_in, 16)
                        sp.dma_start(bk_col[:], bk.rearrange("(t p) -> p t", p=P)).then_inc(small_in, 16)
                    sp.dma_start(bv_row[:], bv.rearrange("(a d) -> a d", a=1).to_broadcast([P, D])).then_inc(small_in, 16)
                    sp.dma_start(bo_row[:], bo.rearrange("(a d) -> a d", a=1).to_broadcast([P, D])).then_inc(small_in, 16)
            blocks(sp, step, first=0, counters=[(next_part, 8 * LOOP_FROM)])
            for s in y_out:
                sp.wait_ge(s, 16 * 2 * B)

        @block.gpsimd
        def _(pool):
            next_aggr = Counter(pool, "next_aggr")
            next_adj = [Counter(pool, f"next_adj{i}", 16) for i in range(2)]
            nc.gpsimd.memset(ident[:], 0.0).then_inc(ident_done, 1)
            nc.gpsimd.memset(minus_half[:], -0.5).then_inc(ident_done, 1)
            pool.wait_ge(ident_done, 2)
            nc.gpsimd.affine_select(out=ident[:], in_=ident[:], compare_op=ALU.not_equal, fill=1.0, base=0,
                                    pattern=[[-1, P]], channel_multiplier=1).then_inc(ident_done, 1)
            pool.wait_ge(ident_done, 3)
            nc.gpsimd.tensor_copy(ident_b[:], ident[:]).then_inc(ident_done, 1)
            pool.wait_ge(small_in, 64)

            def form_rstd(b, t):
                if have(b):
                    pool.wait_ge(aggr_done, due(4 * b + t + 1) if known(b) else next_aggr.reg)
                    if not known(b):
                        next_aggr.advance()
                    nc.gpsimd.tensor_scalar(var_eps[:, t % 2, :], mean_var[:, t % 2, 1:2], LN_EPS, None, ALU.add
                                            ).then_inc(var_done, 1)
                    pool.wait_ge(var_done, due(4 * b + t + 1))
                    nc.gpsimd.tensor_tensor(rstd[:, t % 2, :], var_eps[:, t % 2, :], minus_half[:], ALU.pow
                                            ).then_inc(rstd_done, 1)

            def form_bias(b, t):
                if have(b):
                    pool.wait_ge(m_turned, due(4 * b))
                    pool.wait_ge(masked_max, due(64 * (b - 1) + 48 + 4 * t + 4))
                    pool.wait_ge(adj_in[t % 2], due(16 * (2 * b + t // 2 + 1)) if known(b) else next_adj[t % 2].reg)
                    if not known(b):
                        next_adj[t % 2].advance()
                    nc.gpsimd.tensor_scalar(bias_q[:, t, :], adj_tile[:, t % 2, :], -MASKED, MASKED, ALU.mult, ALU.add
                                            ).then_inc(bias_done, 1)

            def add_bo(b, t):
                if have(b):
                    pool.wait_ge(y_in[t % 2], due(16 * (2 * b + t // 2 + 1)))
                    nc.gpsimd.tensor_tensor(y_tile[:, t % 2, :], y_tile[:, t % 2, :], bo_row[:], ALU.add
                                            ).then_inc(y_plus_bo, 1)

            def step(k, parity):
                form_rstd(k, 2)
                add_bo(k - 2, 2)
                form_rstd(k, 3)
                add_bo(k - 2, 3)
                for t in range(NT):
                    form_bias(k, t)
                for t in range(2):
                    add_bo(k - 1, t)
                for t in range(2):
                    form_rstd(k + 1, t)

            blocks(pool, step, counters=[(next_aggr, 4 * LOOP_FROM + 3)] + [(c, 16 * (2 * LOOP_FROM + 1)) for c in next_adj])

        @block.scalar
        def _(act):
            def wait_stack_loaded(k, i):
                kind, n = QK_ORDER[i]
                if have(k):
                    act.wait_ge(stack_in[kind], due(192 * (4 * k + n + 1)))

            nc.scalar.preload_act_table_set("natural_log_exp_and_others")
            for n in range(4):
                w = "qkvo"[n]
                act.wait_ge(w_in[w], 16)
                nc.scalar.activation(w_hi[w][:], probs[:, 4 * (n % 2):4 * (n % 2) + 4, :], ACT.Identity).then_inc(w_hi_done, 1)
            act.wait_ge(w_lo_done, 4)
            act.wait_ge(small_in, 64)

            def step(k, parity):
                for u in range(SLOTS):
                    b, n = pass2(k, u)
                    if have(b):
                        if n % 4 == 0:
                            act.wait_ge(pv_done, due(16 * b + n // 4 - 1))
                        act.wait_ge(scores2, due(64 * b + n + 1))
                        nc.scalar.activation(probs[:, n % P_RING, :], ps2[:, n % 2, :], ACT.Exp, scale=SCALE
                                             ).then_inc(exp2_done, 1)
                    b, n = pass1(k, u - 1) if u else pass1(k - 1, SLOTS - 1)
                    if have(b):
                        g, qt, j = n // 16, n % 16 // 4, n % 4
                        col = 4 * j + qt
                        act.wait_ge(masked_max, due(64 * b + n + 1))
                        nc.scalar.activation(ps1[:, n % 2, :], ps1[:, n % 2, :], ACT.Exp, scale=-1.0,
                                             bias=neg_max[:, g % 2, col:col + 1],
                                             accum_out=exp_sum[:, g % 2, col:col + 1]).then_inc(exp1_done, 1)
                        if n % 16 == 15:
                            act.wait_ge(exp1_done, due(64 * b + n + 1))
                            act.wait_ge(c_sum_done, due(4 * b + g))
                            nc.scalar.activation(ln_sum[:], exp_sum[:, g % 2, :], ACT.Ln).then_inc(ln_done, 1)
                    if u in O_EVAC and have(k - 1):
                        g = O_EVAC[u]
                        act.wait_ge(pv_done, due(16 * (k - 1) + 4 * g + 4))
                        if g == 0:
                            act.wait_ge(out_done, due(4 * (k - 1)))
                        nc.scalar.activation(oT_hi[:, g, :], psO[:], ACT.Identity).then_inc(o_hi_done, 1)
                    for kind, n, rel in TURNS.get(u, ()):
                        if kind == "h" and have(k):
                            act.wait_ge(h_turned, due(4 * k + n + 1))
                            if n == 0:
                                act.wait_ge(qkv_done, due(12 * k))
                            nc.scalar.activation(hT_hi[:, :, P * n:P * n + P], psT[:].rearrange("p (t q) -> p t q", q=P),
                                                 ACT.Relu).then_inc(h_hi_done, 1)
                    if u % 4 == 0:
                        T, b = (u // 4 - 1, k) if u else (15, k - 1)
                        kind, n = TILES[T]
                        if kind in "qk" and have(b):
                            i = QK_ORDER.index((kind, n))
                            act.wait_ge(qkv_done, due(12 * b + QKV_TILES.index((kind, n)) + 1))
                            if i:
                                wait_stack_loaded(b, i - 1)
                            else:
                                wait_stack_loaded(b - 1, 7)
                            bias = (bq_col if kind == "q" else bk_col)[:, n:n + 1]
                            nc.scalar.activation(part_hi[:], psP[:, T % 2, :], ACT.Identity, bias=bias).then_inc(qk_hi_done, 1)

            blocks(act, step)

        @block.vector
        def _(dve):
            next_scores, next_stats = Counter(dve, "next_scores"), Counter(dve, "next_stats")
            nc.vector.memset(k_stack[STACK:STACK + 2].bitcast(F32), 1.0)

            def ln_stats(b, t):
                if have(b):
                    dve.wait_ge(x_in[t % 2], due(16 * (2 * b + t // 2 + 1)))
                    dve.wait_ge(aggr_done, due(4 * b + t))
                    nc.vector.bn_stats(stats[:], x_tile[:, t % 2, :]).then_inc(stats_done, 1)
                    dve.wait_ge(norm_done, due(4 * b + t - 1))
                    dve.wait_ge(stats_done, due(4 * b + t + 1) if known(b) else next_stats.reg)
                    if not known(b):
                        next_stats.advance()
                    nc.vector.bn_aggr(mean_var[:, t % 2, :], stats[:]).then_inc(aggr_done, 1)

            def normalise(b, t):
                if have(b):
                    dve.wait_ge(rstd_done, due(4 * b + t + 1))
                    nc.vector.tensor_scalar(x_tile[:, t % 2, :], x_tile[:, t % 2, :], mean_var[:, t % 2, 0:1],
                                            rstd[:, t % 2, :], ALU.subtract, ALU.mult).then_inc(norm_done, 1)

            def form_c(b, g):
                dve.wait_ge(ln_done, due(4 * b + g + 1))
                nc.vector.tensor_tensor(c_all[:], neg_max[:, g % 2, :], ln_sum[:], ALU.subtract).then_inc(c_sum_done, 1)
                dve.wait_ge(c_sum_done, due(4 * b + g + 1))
                dve.wait_ge(c_turned, due(4 * b + g))
                nc.vector.tensor_scalar(c_parts[:, 0, :], c_all[:], 1.0 / SCALE, None, ALU.mult).then_inc(c_hi_done, 1)
                dve.wait_ge(c_hi_done, due(4 * b + g + 1))
                nc.vector.scalar_tensor_tensor(out=c_parts[:, 1, :], in0=c_all[:], scalar=1.0 / SCALE,
                                               in1=c_parts[:, 0, :].bitcast(F32), op0=ALU.mult, op1=ALU.subtract
                                               ).then_inc(c_lo_done, 1)

            def take_turn(k, kind, n, rel):
                b = k + rel
                if not have(b):
                    return
                if kind == "h":
                    dve.wait_ge(h_hi_done, due(4 * b + n + 1))
                    nc.vector.scalar_tensor_tensor(
                        out=hT_lo[:, :, P * n:P * n + P], in0=psT[:].rearrange("p (t q) -> p t q", q=P), scalar=0.0,
                        in1=hT_hi[:, :, P * n:P * n + P].bitcast(F32), op0=ALU.max, op1=ALU.subtract
                    ).then_inc(h_lo_done, 1)
                elif kind == "m":
                    dve.wait_ge(m_turned, due(4 * b + n + 1))
                    dve.wait_ge(scores2, due(64 * (b - 1) + 48 + 4 * n + 4))
                    nc.vector.tensor_copy(bias_k[:, n, :], psT[:, 0:S // 2].bitcast(BF16)).then_inc(m_done, 1)
                else:
                    dve.wait_ge(c_turned, due(4 * b + n + 1))
                    dve.wait_ge(c_in, due(32 * (4 * b + n)))
                    nc.vector.tensor_copy(c_rows[:], psT[0:32, 0:P]).then_inc(c_rows_done, 1)

            def step(k, parity):
                for u in range(SLOTS):
                    if u in C_AT:
                        g, rel = C_AT[u]
                        if have(k + rel):
                            form_c(k + rel, g)
                    b, n = pass1(k, u)
                    if have(b):
                        g, qt, j = n // 16, n % 16 // 4, n % 4
                        col = 4 * j + qt
                        if g == 0 and j == 0:
                            dve.wait_ge(bias_done, due(4 * b + qt + 1))
                        dve.wait_ge(scores1, due(64 * b + n + 1) if known(b) else next_scores.reg)
                        if not known(b):
                            next_scores.advance()
                        nc.vector.tensor_tensor_reduce(ps1[:, n % 2, :], ps1[:, n % 2, :], bias_q[:, qt, :], -SCALE, 3.0e38,
                                                       ALU.add, ALU.min, neg_max[:, g % 2, col:col + 1]
                                                       ).then_inc(masked_max, 1)
                    for kind, n, rel in TURNS.get(u, ()):
                        take_turn(k, kind, n, rel)
                    if u in O_EVAC and have(k - 1):
                        g = O_EVAC[u]
                        dve.wait_ge(o_hi_done, due(4 * (k - 1) + g + 1))
                        nc.vector.tensor_tensor(oT_lo[:, g, :], psO[:], oT_hi[:, g, :].bitcast(F32), ALU.subtract
                                                ).then_inc(o_lo_done, 1)
                    if u % 4 == 0:
                        T, kb = (u // 4 - 1, k) if u else (15, k - 1)
                        kind, n = TILES[T]
                        b = kb - 2 if kind == "o" else kb
                        if have(b) and kind == "o":
                            dve.wait_ge(out_done, due(4 * b + n + 1))
                            dve.wait_ge(y_plus_bo, due(4 * b + n + 1))
                            nc.vector.tensor_tensor(y_tile[:, n % 2, :], psP[:, T % 2, :], y_tile[:, n % 2, :], ALU.add
                                                    ).then_inc(y_done, 1)
                        elif have(b) and kind == "v":
                            dve.wait_ge(qkv_done, due(12 * b + QKV_TILES.index((kind, n)) + 1))
                            dve.wait_ge(pv_done, due(16 * (b - 1)))
                            nc.vector.tensor_tensor(v_sb[:, parity, n, :], psP[:, T % 2, :], bv_row[:], ALU.add
                                                    ).then_inc(v_done, 1)
                        elif have(b):
                            i = QK_ORDER.index((kind, n))
                            dve.wait_ge(qk_hi_done, due(8 * b + i + 1))
                            bias = (bq_col if kind == "q" else bk_col)[:, n:n + 1]
                            nc.vector.scalar_tensor_tensor(out=part_lo[:], in0=psP[:, T % 2, :], scalar=bias,
                                                           in1=part_hi[:].bitcast(F32), op0=ALU.add, op1=ALU.subtract
                                                           ).then_inc(qk_lo_done, 1)
                    if u == 4: ln_stats(k, 2)
                    if u == 7: normalise(k, 2)
                    if u == 8: ln_stats(k, 3)
                    if u == 12: normalise(k, 3)
                    if u == 52: ln_stats(k + 1, 0)
                    if u == 54: ln_stats(k + 1, 1)
                    if u == 56: normalise(k + 1, 0)
                    if u == 58: normalise(k + 1, 1)

            for n in range(4):
                w = "qkvo"[n]
                dve.wait_ge(w_hi_done, n + 1)
                nc.vector.tensor_tensor(w_lo[w][:], probs[:, 4 * (n % 2):4 * (n % 2) + 4, :], w_hi[w][:].bitcast(F32),
                                        ALU.subtract).then_inc(w_lo_done, 1)
            dve.wait_ge(small_in, 64)
            blocks(dve, step, counters=[(next_scores, 64 * (LOOP_FROM - 1) + SLOTS - S1_AT + 1),
                                        (next_stats, 4 * LOOP_FROM + 3)])

        @block.tensor
        def _(pe):
            def wait_tile_out(k, T):
                kind, n = TILES[T]
                if not have(k - 2 if kind == "o" else k):
                    return
                if kind == "o":
                    pe.wait_ge(y_done, due(4 * (k - 2) + n + 1))
                elif kind == "v":
                    pe.wait_ge(v_done, due(4 * k + n + 1))
                else:
                    i = QK_ORDER.index((kind, n))
                    pe.wait_ge(qk_hi_done, due(8 * k + i + 1))
                    pe.wait_ge(qk_lo_done, due(8 * k + i + 1))

            def wait_turn_out(k, i):
                kind, n, rel = TURN_LIST[i]
                if not have(k + rel):
                    return
                if kind == "h":
                    pe.wait_ge(h_hi_done, due(4 * k + n + 1))
                    pe.wait_ge(h_lo_done, due(4 * k + n + 1))
                elif kind == "m":
                    pe.wait_ge(m_done, due(4 * k + n + 1))
                else:
                    pe.wait_ge(c_rows_done, due(4 * (k + rel) + n + 1))

            def three_products(acc, w_h, w_l, m_h, m_l, kt):
                nc.tensor.matmul(acc, w_h, m_h, start=(kt == 0), stop=False)
                nc.tensor.matmul(acc, w_h, m_l, start=False, stop=False)
                return nc.tensor.matmul(acc, w_l, m_h, start=False, stop=(kt == NT - 1))

            def project(k, u):
                T, kt = u // 4, u % 4
                kind, n = TILES[T]
                b = k - 2 if kind == "o" else k
                if not have(b):
                    return
                if kt == 0:
                    wait_tile_out(*((k, T - 2) if T >= 2 else (k - 1, T + 14)))
                    if T == 0:
                        pe.wait_ge(o_hi_done, due(4 * b + 4))
                        pe.wait_ge(o_lo_done, due(4 * b + 4))
                    if T == 4:
                        pe.wait_ge(h_hi_done, due(4 * b + 4))
                        pe.wait_ge(h_lo_done, due(4 * b + 4))
                acc = psP[:, T % 2, :]
                rows = slice(P * n, P * n + P)
                if kind in "qk":
                    last = three_products(acc, w_hi[kind][:, kt, rows], w_lo[kind][:, kt, rows],
                                          hT_hi[:, kt, :], hT_lo[:, kt, :], kt)
                elif kind == "v":
                    last = three_products(acc, hT_hi[:, kt, rows], hT_lo[:, kt, rows],
                                          w_hi["v"][:, kt, :], w_lo["v"][:, kt, :], kt)
                else:
                    last = three_products(acc, oT_hi[:, kt, rows], oT_lo[:, kt, rows],
                                          w_hi["o"][:, kt, :], w_lo["o"][:, kt, :], kt)
                if kt == NT - 1:
                    last.then_inc(out_done if kind == "o" else qkv_done, 1)

            def turn(k, kind, n, rel):
                b = k + rel
                if not have(b):
                    return
                i = TURN_LIST.index((kind, n, rel))
                wait_turn_out(*((k, i - 1) if i else (k - 1, len(TURN_LIST) - 1)))
                if kind == "h":
                    pe.wait_ge(norm_done, due(4 * b + n + 1))
                    for t in range(NT):
                        last = nc.tensor.transpose(psT[:, P * t:P * t + P], x_tile[:, n % 2, P * t:P * t + P], ident[:])
                    last.then_inc(h_turned, 1)
                elif kind == "m":
                    pe.wait_ge(bias_done, due(4 * b + 4))
                    for t in range(NT):
                        last = nc.tensor.transpose(psT[:, 64 * t:64 * t + 64].bitcast(BF16),
                                                   bias_q[:, t, P * n:P * n + P], ident_b[:])
                    last.then_inc(m_turned, 1)
                else:
                    pe.wait_ge(c_lo_done, due(4 * b + n + 1))
                    nc.tensor.transpose(psT[0:32, 0:P], c_parts[:].rearrange("p a n -> p (a n)").bitcast(F32), ident[:]
                                        ).then_inc(c_turned, 1)

            def step(k, parity):
                for u in range(SLOTS):
                    b, n = pass1(k, u)
                    if have(b):
                        g, qt, j = n // 16, n % 16 // 4, n % 4
                        if n % 16 == 0:
                            pe.wait_ge(stack_in["q"], due(192 * (4 * b + g + 1)))
                            pe.wait_ge(stack_in["k"], due(192 * (4 * b + g + 1)))
                        pe.wait_ge(exp1_done, due(64 * b + n - 1))
                        nc.tensor.matmul(ps1[:, n % 2, :], q_stack[0:STACK, g, j, P * qt:P * qt + P],
                                         k_stack[0:STACK, g, j, :], start=True, stop=True).then_inc(scores1, 1)
                    b, n = pass2(k, u)
                    if have(b):
                        g, kt, j = n // 16, n % 16 // 4, n % 4
                        if n % 16 == 0:
                            pe.wait_ge(c_in, due(32 * (4 * b + g + 1)))
                        if g == 0 and j == 0:
                            pe.wait_ge(m_done, due(4 * b + kt + 1))
                        pe.wait_ge(exp2_done, due(64 * b + n - 1))
                        nc.tensor.matmul(ps2[:, n % 2, :], k_stack[:, g, j, P * kt:P * kt + P], q_stack[:, g, j, :],
                                         start=True, stop=False)
                        nc.tensor.matmul(ps2[:, n % 2, :], ident_b[:], bias_k[:, kt, :], start=False, stop=True
                                         ).then_inc(scores2, 1)
                    project(k, u)
                    if u % 4 == 2 and have(k - 1):
                        b, n = k - 1, u // 4
                        g, kt = n // 4, n % 4
                        if kt == 0:
                            pe.wait_ge(o_hi_done, due(4 * b + g))
                            pe.wait_ge(o_lo_done, due(4 * b + g))
                        if g == 0:
                            pe.wait_ge(v_done, due(4 * b + kt + 1))
                        pe.wait_ge(exp2_done, due(64 * b + 4 * n + 4))
                        for j in range(GROUP):
                            at = DH * (GROUP * g + j)
                            last = nc.tensor.matmul(psO[32 * j:32 * j + 32, :], v_sb[:, 1 - parity, kt, at:at + DH],
                                                    probs[:, (4 * n + j) % P_RING, :], start=(kt == 0), stop=(kt == NT - 1))
                        last.then_inc(pv_done, 1)
                    for kind, n, rel in TURNS.get(u, ()):
                        turn(k, kind, n, rel)

            pe.wait_ge(ident_done, 4)
            pe.wait_ge(w_lo_done, 4)
            blocks(pe, step)


_INS = ['x', 'adj', 'L0_gnn_Wq', 'L0_gnn_bq', 'L0_gnn_Wk', 'L0_gnn_bk', 'L0_gnn_Wv', 'L0_gnn_bv', 'L0_gnn_Wo', 'L0_gnn_bo']


def kernel(**inputs):
    import numpy as _np
    import concourse.bacc as _bacc
    from concourse import mybir as _mybir
    from concourse.bass_utils import run_bass_kernel_spmd as _run

    nc = _bacc.Bacc("TRN2", target_bir_lowering=False, num_devices=1, dynamic_dma_scratch_size=256)
    arrays, args = {}, []
    for name in _INS:
        a = _np.ascontiguousarray(inputs[name])
        arrays[f"in_{name}_dram"] = a
        args.append(nc.dram_tensor(f"in_{name}_dram", a.shape, _mybir.dt.from_np(a.dtype), kind="ExternalInput").ap())
    out = nc.dram_tensor("out_0_dram", inputs["x"].shape, _mybir.dt.float32, kind="ExternalOutput").ap()
    attention_block(nc, *args, out)
    r = _run(nc, [arrays], core_ids=[0])
    return r.results[0]["out_0_dram"]
```

```python
from contextlib import ExitStack

import concourse.bass as bass
from concourse import mybir

ALU = mybir.AluOpType
ACT = mybir.ActivationFunctionType
F32 = mybir.dt.float32
F32R = mybir.dt.float32r
BF16 = mybir.dt.bfloat16
I32 = mybir.dt.int32

P = 128
HEADS = 16
GROUP = 4
NT = 4
SLOTS = 64
S1_AT, S2_AT = 35, 60
ADJ_AT = (17, 24, 30, 36)
BIAS_AT = (24, 30, 36, 46)
SPLIT_AT = (2, 8, 19, 25)
MASKED = -2.0 ** 100
LN_EPS = 1e-5
STACK = 96
P_RING = 8
VECTOR_MASKED = (1, 3, 5, 7)

TILES = ([("o", t) for t in range(4)]
         + [("q", 0), ("k", 0), ("v", 0), ("q", 1), ("k", 1), ("v", 1), ("q", 2), ("k", 2),
            ("v", 2), ("v", 3), ("q", 3), ("k", 3)])
QKV_TILES = [x for x in TILES if x[0] != "o"]
QK_ORDER = [x for x in TILES if x[0] in "qk"]
TURNS = {1: [("h", 0, 0)], 5: [("h", 1, 0)], 8: [("c", 1, -1)], 10: [("h", 2, 0)], 13: [("h", 3, 0)],
         24: [("c", 2, -1)], 40: [("c", 3, -1)], 53: [("m", 0, 0)], 56: [("c", 0, 0)], 61: [("m", 1, 0)]}
RING = []
for _u in range(SLOTS):
    _c = [x for x in TURNS.get(_u, ()) if x[0] == "c"]
    RING += _c + [("s", _u)] + [x for x in TURNS.get(_u, ()) if x not in _c]
O_HI_AT = {16: 0, 31: 1, 47: 2, 63: 3}
O_LO_AT = {17: 0, 32: 1, 48: 2, 63: 3}
C_AT = {4: (1, -1), 20: (2, -1), 36: (3, -1), 52: (0, 0)}


def attention_block(nc, x, adj, Wq, bq, Wk, bk, Wv, bv, Wo, bo, out):
    B, S, D = x.shape
    DH = D // HEADS
    SCALE = float(DH) ** -0.5
    assert S == NT * P and D == NT * P and DH * GROUP == P
    LOOP_FROM, LOOP_TO = 2, B - 2
    assert (LOOP_TO - LOOP_FROM) % 2 == 0

    x_rows = x.rearrange("b (t p) d -> (b t) p d", p=P)
    adj_rows = adj.rearrange("b (t p) d -> (b t) p d", p=P)
    out_rows = out.rearrange("b (t p) d -> (b t) p d", p=P)

    with ExitStack() as ctx:
        def sb(name, shape, dt):
            return ctx.enter_context(nc.sbuf_tensor(name, shape, dt))

        def sem(name):
            return ctx.enter_context(nc.semaphore(name))

        w_hi = {n: sb(f"w{n}_hi", [P, NT, D], F32R) for n in "qkvo"}
        w_lo = {n: sb(f"w{n}_lo", [P, NT, D], F32R) for n in "qkvo"}
        hT_hi = sb("hT_hi", [P, NT, S], F32R)
        hT_lo = sb("hT_lo", [P, NT, S], F32R)
        q_stack = sb("q_stack", [STACK + 2, NT, GROUP, S], F32R)
        k_stack = sb("k_stack", [STACK + 2, NT, GROUP, S], F32R)
        v_sb = sb("v_sb", [P, 2, NT, D], F32)
        oT_hi = sb("oT_hi", [P, NT, S], F32R)
        oT_lo = sb("oT_lo", [P, NT, S], F32R)
        x_tile = sb("x_tile", [P, 2, D], F32)
        adj_tile = sb("adj_tile", [P, S], I32)
        bias_q = sb("bias_q", [P, NT, S], BF16)
        bias_k = sb("bias_k", [P, NT, S], BF16)
        probs = sb("probs", [P, P_RING, S], F32)
        part_hi = sb("part_hi", [P, 2, S], F32R)
        part_lo = sb("part_lo", [P, 2, S], F32R)
        y_tile = sb("y_tile", [P, 2, D], F32)
        bq_col = sb("bq_col", [P, NT], F32)
        bk_col = sb("bk_col", [P, NT], F32)
        bv_col = sb("bv_col", [P, NT], F32)
        bo_row = sb("bo_row", [P, D], F32)
        ident = sb("ident", [P, P], F32)
        ident_b = sb("ident_b", [P, P], BF16)
        minus_half = sb("minus_half", [P, 1], F32)
        stats = sb("stats", [P, 6], F32)
        mean_var = sb("mean_var", [P, 2, 2], F32)
        var_eps = sb("var_eps", [P, 2, 1], F32)
        rstd = sb("rstd", [P, 2, 1], F32)
        neg_max = sb("neg_max", [P, 2, 16], F32)
        exp_sum = sb("exp_sum", [P, 2, 16], F32)
        ln_sum = sb("ln_sum", [P, 16], F32)
        c_all = sb("c_all", [P, 16], F32)
        c_parts = sb("c_parts", [P, 2, 16], F32R)
        c_rows = sb("c_rows", [32, P], F32R)

        ps1 = ctx.enter_context(nc.psum_tensor("ps1", [P, 3, S], F32))
        ps2 = ctx.enter_context(nc.psum_tensor("ps2", [P, 2, S], F32))
        psP = ctx.enter_context(nc.psum_tensor("psP", [P, 2, S], F32))
        psO = ctx.enter_context(nc.psum_tensor("psO", [P, S], F32))

        w_in = {n: sem(f"w{n}_in") for n in "qkvo"}
        small_in = sem("small_in")
        w_hi_done, w_lo_done = sem("w_hi_done"), sem("w_lo_done")
        ident_done = sem("ident_done")
        x_in = [sem("x_in0"), sem("x_in1")]
        adj_in = sem("adj_in")
        y_in = [sem("y_in0"), sem("y_in1")]
        y_out = [sem("y_out0"), sem("y_out1")]
        stack_in = {"q": sem("q_stack_in"), "k": sem("k_stack_in")}
        c_in = sem("c_in")
        stats_done, aggr_done = sem("stats_done"), sem("aggr_done")
        var_done, rstd_done, norm_done = sem("var_done"), sem("rstd_done"), sem("norm_done")
        h_turned, h_hi_done, h_lo_done = sem("h_turned"), sem("h_hi_done"), sem("h_lo_done")
        bias_done = sem("bias_done")
        m_turned, m_done = sem("m_turned"), sem("m_done")
        qkv_done, out_done = sem("qkv_done"), sem("out_done")
        qk_hi_done, qk_lo_done = sem("qk_hi_done"), sem("qk_lo_done")
        v_done = sem("v_done")
        scores1, masked_max, exp1_done = sem("scores1"), sem("masked_max"), sem("exp1_done")
        ln_done, c_sum_done, c_hi_done, c_lo_done = sem("ln_done"), sem("c_sum_done"), sem("c_hi_done"), sem("c_lo_done")
        c_turned, c_rows_done = sem("c_turned"), sem("c_rows_done")
        scores2, exp2_done = sem("scores2"), sem("exp2_done")
        probs_masked = sem("probs_masked")
        pv_done, o_hi_done, o_lo_done = sem("pv_done"), sem("o_hi_done"), sem("o_lo_done")
        y_plus_bo, y_done = sem("y_plus_bo"), sem("y_done")

        def known(b):
            return isinstance(b, int)

        def have(b):
            return not known(b) or 0 <= b < B

        def due(count):
            return max(count, 0) if known(count) else count

        class Counter:
            def __init__(self, eng, name, step=1):
                self.eng, self.reg, self.step = eng, eng.alloc_register(name), step

            def start(self, value):
                self.eng.reg_mov(self.reg, value)

            def advance(self):
                self.eng.reg_add(self.reg, self.reg, self.step)

        def pass1(k, u):
            return (k, u - S1_AT) if u >= S1_AT else (k - 1, u + SLOTS - S1_AT)

        def bank1(item):
            return ps1[:, RING.index(item) % 3, :]

        def pass2(k, u):
            return (k, u - S2_AT) if u >= S2_AT else (k - 1, u + SLOTS - S2_AT)

        def masked_before(n):
            return n // 8 * len(VECTOR_MASKED) + sum(i < n % 8 for i in VECTOR_MASKED)

        MASKED_ALL = masked_before(SLOTS)

        def blocks(eng, block, first=-1, counters=()):
            for k in range(first, LOOP_FROM):
                block(k, k % 2)
            for counter, value in counters:
                counter.start(value)
            with eng.Fori(LOOP_FROM, LOOP_TO, 2) as k:
                block(k, 0)
                block(k + 1, 1)
            for k in range(LOOP_TO, B + 2):
                block(k, k % 2)

        block = ctx.enter_context(nc.Block())

        @block.sync
        def _(sp):
            next_part = Counter(sp, "next_part")

            def load_x(b, t):
                if have(b):
                    row = 4 * b + t
                    sp.wait_ge(h_turned, due(4 * b + t - 1))
                    sp.dma_start(x_tile[:, t % 2, :], x_rows[bass.ds(row, 1)].rearrange("a p d -> (a p) d")
                                 ).then_inc(x_in[t % 2], 16)

            def load_adj(b, t):
                if have(b):
                    row = 4 * b + t
                    sp.wait_ge(bias_done, due(4 * b + t))
                    sp.dma_start(adj_tile[:], adj_rows[bass.ds(row, 1)].rearrange("a p d -> (a p) d")
                                 ).then_inc(adj_in, 16)

            def load_y(b, t):
                if have(b):
                    row = 4 * b + t
                    sp.wait_ge(y_out[t % 2], due(16 * (2 * b + t // 2)))
                    sp.dma_start(y_tile[:, t % 2, :], x_rows[bass.ds(row, 1)].rearrange("a p d -> (a p) d")
                                 ).then_inc(y_in[t % 2], 16)

            def store_y(b, t):
                if have(b):
                    row = 4 * b + t
                    sp.wait_ge(y_done, due(4 * b + t + 1))
                    sp.dma_start(out_rows[bass.ds(row, 1)].rearrange("a p d -> (a p) d"), y_tile[:, t % 2, :]
                                 ).then_inc(y_out[t % 2], 16)

            def load_stack(b, i):
                if not have(b):
                    return
                kind, g = QK_ORDER[i]
                stack = q_stack if kind == "q" else k_stack
                lo_row = 64 if kind == "q" else 32
                sp.wait_ge(scores2, due(64 * (b - 1) + 16 * (g + 1)))
                sp.wait_ge(qk_hi_done, due(8 * b + i + 1) if known(b) else next_part.reg)
                hi_rows = [r for r in (0, 32, 64) if r != lo_row]
                for j in range(GROUP):
                    sp.dma_start(stack[hi_rows[0]:hi_rows[0] + 32, g, j, :].bitcast(F32),
                                 part_hi[32 * j:32 * j + 32, i % 2, :].bitcast(F32)).then_inc(stack_in[kind], 16)
                sp.wait_ge(qk_lo_done, due(8 * b + i + 1) if known(b) else next_part.reg)
                for j in range(GROUP):
                    sp.dma_start(stack[lo_row:lo_row + 32, g, j, :].bitcast(F32),
                                 part_lo[32 * j:32 * j + 32, i % 2, :].bitcast(F32)).then_inc(stack_in[kind], 16)
                for j in range(GROUP):
                    sp.dma_start(stack[hi_rows[1]:hi_rows[1] + 32, g, j, :].bitcast(F32),
                                 part_hi[32 * j:32 * j + 32, i % 2, :].bitcast(F32)).then_inc(stack_in[kind], 16)
                if not known(b):
                    next_part.advance()

            def load_weight(n, w):
                at = 4 * ("qkvo".index(n) % 2)
                if n in "vo":
                    sp.wait_ge(w_lo_done, "qkvo".index(n) - 1)
                sp.dma_start(probs[:, at:at + 4, :], w.rearrange("(t p) d -> p t d", p=P)).then_inc(w_in[n], 16)

            def step(k, parity):
                for u in range(SLOTS):
                    if u == 1: load_x(k, 2)
                    if u == 5: load_x(k, 3)
                    if known(k) and k == 0 and u == 2: load_weight("v", Wv)
                    if known(k) and k == 0 and u == 6: load_weight("o", Wo)
                    if u == 12: load_x(k + 1, 0)
                    if u == 15: load_x(k + 1, 1)
                    if u in ADJ_AT: load_adj(k, ADJ_AT.index(u))
                    if u < 20 and u % 4 == 1 and u >= 5: store_y(k - 2, (u - 5) // 4)
                    if u in (7, 11): load_y(k - 2, (u + 1) // 4)
                    if u in (44, 46): load_y(k - 1, (u - 44) // 2)
                    if u % 4 == 1:
                        T, b = (u // 4 - 1, k) if u >= 4 else (15, k - 1)
                        if TILES[T][0] in "qk":
                            load_stack(b, QK_ORDER.index(TILES[T]))

            step(-1, 1)
            load_weight("q", Wq)
            load_weight("k", Wk)
            with nc.allow_non_contiguous_dma(reason="three bias vectors, once"):
                sp.dma_start(bq_col[:], bq.rearrange("(t p) -> p t", p=P)).then_inc(small_in, 16)
                sp.dma_start(bk_col[:], bk.rearrange("(t p) -> p t", p=P)).then_inc(small_in, 16)
                sp.dma_start(bv_col[:], bv.rearrange("(t p) -> p t", p=P)).then_inc(small_in, 16)
            sp.dma_start(bo_row[:], bo.rearrange("(a d) -> a d", a=1).to_broadcast([P, D])).then_inc(small_in, 16)
            blocks(sp, step, first=0, counters=[(next_part, 8 * LOOP_FROM)])
            for s in y_out:
                sp.wait_ge(s, 16 * 2 * B)

        @block.gpsimd
        def _(pool):
            next_aggr = Counter(pool, "next_aggr")
            nc.gpsimd.memset(ident[:], 0.0).then_inc(ident_done, 1)
            nc.gpsimd.memset(minus_half[:], -0.5).then_inc(ident_done, 1)
            pool.wait_ge(ident_done, 2)
            nc.gpsimd.affine_select(out=ident[:], in_=ident[:], compare_op=ALU.not_equal, fill=1.0, base=0,
                                    pattern=[[-1, P]], channel_multiplier=1).then_inc(ident_done, 1)
            pool.wait_ge(ident_done, 3)
            nc.gpsimd.tensor_copy(ident_b[:], ident[:]).then_inc(ident_done, 1)

            def form_rstd(b, t):
                if have(b):
                    pool.wait_ge(aggr_done, due(4 * b + t + 1) if known(b) else next_aggr.reg)
                    if not known(b):
                        next_aggr.advance()
                    nc.gpsimd.tensor_scalar(var_eps[:, t % 2, :], mean_var[:, t % 2, 1:2], LN_EPS, None, ALU.add
                                            ).then_inc(var_done, 1)
                    pool.wait_ge(var_done, due(4 * b + t + 1))
                    nc.gpsimd.tensor_tensor(rstd[:, t % 2, :], var_eps[:, t % 2, :], minus_half[:], ALU.pow
                                            ).then_inc(rstd_done, 1)

            def add_bo(b, t):
                if have(b):
                    pool.wait_ge(y_in[t % 2], due(16 * (2 * b + t // 2 + 1)))
                    nc.gpsimd.tensor_tensor(y_tile[:, t % 2, :], y_tile[:, t % 2, :], bo_row[:], ALU.add
                                            ).then_inc(y_plus_bo, 1)

            def step(k, parity):
                form_rstd(k, 2)
                add_bo(k - 2, 2)
                form_rstd(k, 3)
                add_bo(k - 2, 3)
                for t in range(2):
                    form_rstd(k + 1, t)
                if known(k) and k == 0:
                    pool.wait_ge(small_in, 64)
                for t in range(2):
                    add_bo(k - 1, t)

            blocks(pool, step, counters=[(next_aggr, 4 * LOOP_FROM + 3)])

        @block.scalar
        def _(act):
            def wait_stack_loaded(k, i):
                kind, n = QK_ORDER[i]
                if have(k):
                    act.wait_ge(stack_in[kind], due(192 * (4 * k + n + 1)))

            def load_c(b, g):
                if have(b):
                    act.wait_ge(c_rows_done, due(4 * b + g + 1))
                    for part in range(2):
                        act.dma_start(q_stack[STACK + part:STACK + part + 1, g, :, :].rearrange("a j (t q) -> a (j t) q", q=P).bitcast(F32),
                                      c_rows[16 * part:16 * part + 16, :].bitcast(F32)).then_inc(c_in, 16)

            nc.scalar.preload_act_table_set("natural_log_exp_and_others")

            def split_weight(n):
                w = "qkvo"[n]
                act.wait_ge(w_in[w], 16)
                nc.scalar.activation(w_hi[w][:], probs[:, 4 * (n % 2):4 * (n % 2) + 4, :], ACT.Identity).then_inc(w_hi_done, 1)

            def step(k, parity):
                for u in range(SLOTS):
                    if known(k) and k == 0:
                        if u in SPLIT_AT:
                            split_weight(SPLIT_AT.index(u))
                        if u == 16:
                            act.wait_ge(small_in, 64)
                        if u == 59:
                            act.wait_ge(w_lo_done, 4)
                    b, n = pass1(k, u - 1) if u else pass1(k - 1, SLOTS - 1)
                    if have(b):
                        g, qt, j = n // 16, n % 16 // 4, n % 4
                        col = 4 * j + qt
                        act.wait_ge(masked_max, due(64 * b + n + 1))
                        item = bank1(("s", (u - 1) % SLOTS))
                        nc.scalar.activation(item, item, ACT.Exp, scale=-1.0,
                                             bias=neg_max[:, g % 2, col:col + 1],
                                             accum_out=exp_sum[:, g % 2, col:col + 1]).then_inc(exp1_done, 1)
                        if n % 16 == 15:
                            act.wait_ge(exp1_done, due(64 * b + n + 1))
                            act.wait_ge(c_sum_done, due(4 * b + g))
                            nc.scalar.activation(ln_sum[:], exp_sum[:, g % 2, :], ACT.Ln).then_inc(ln_done, 1)
                    if u in O_HI_AT and have(k - 1):
                        g = O_HI_AT[u]
                        act.wait_ge(pv_done, due(16 * (k - 1) + 4 * g + 4))
                        if g == 0:
                            act.wait_ge(out_done, due(4 * (k - 1)))
                        nc.scalar.activation(oT_hi[:, g, :], psO[:], ACT.Identity, bias=bv_col[:, g:g + 1]).then_inc(o_hi_done, 1)
                    if u % 4 == 0:
                        T, b = (u // 4 - 1, k) if u else (15, k - 1)
                        kind, n = TILES[T]
                        if kind in "qk" and have(b):
                            i = QK_ORDER.index((kind, n))
                            act.wait_ge(qkv_done, due(12 * b + QKV_TILES.index((kind, n)) + 1))
                            wait_stack_loaded(*((b, i - 2) if i >= 2 else (b - 1, i + 6)))
                            bias = (bq_col if kind == "q" else bk_col)[:, n:n + 1]
                            nc.scalar.activation(part_hi[:, i % 2, :], psP[:, T % 2, :], ACT.Identity, bias=bias).then_inc(qk_hi_done, 1)
                    b, n = pass2(k, u)
                    if have(b):
                        if n % 4 == 0:
                            act.wait_ge(pv_done, due(16 * b + n // 4 - 1))
                        act.wait_ge(scores2, due(64 * b + n + 1))
                        nc.scalar.activation(probs[:, n % P_RING, :], ps2[:, n % 2, :], ACT.Exp, scale=SCALE
                                             ).then_inc(exp2_done, 1)
                    for kind, n, rel in TURNS.get(u - 1, ()):
                        if kind == "c":
                            load_c(k + rel, n)
                    for kind, n, rel in TURNS.get(u, ()):
                        if kind == "h" and have(k):
                            act.wait_ge(h_turned, due(4 * k + n + 1))
                            if n == 0:
                                act.wait_ge(qkv_done, due(12 * k))
                            nc.scalar.activation(hT_hi[:, :, P * n:P * n + P], bank1((kind, n, rel)).rearrange("p (t q) -> p t q", q=P),
                                                 ACT.Relu).then_inc(h_hi_done, 1)

            blocks(act, step)

        @block.vector
        def _(dve):
            next_scores, next_stats = Counter(dve, "next_scores"), Counter(dve, "next_stats")
            next_adj = Counter(dve, "next_adj", 16)
            nc.vector.memset(k_stack[STACK:STACK + 2].bitcast(F32), 1.0)

            def wait_stack_loaded(k, i):
                kind, n = QK_ORDER[i]
                if have(k):
                    dve.wait_ge(stack_in[kind], due(192 * (4 * k + n + 1)))

            def ln_stats(b, t):
                if have(b):
                    dve.wait_ge(x_in[t % 2], due(16 * (2 * b + t // 2 + 1)))
                    dve.wait_ge(aggr_done, due(4 * b + t))
                    nc.vector.bn_stats(stats[:], x_tile[:, t % 2, :]).then_inc(stats_done, 1)
                    dve.wait_ge(norm_done, due(4 * b + t - 1))
                    dve.wait_ge(stats_done, due(4 * b + t + 1) if known(b) else next_stats.reg)
                    if not known(b):
                        next_stats.advance()
                    nc.vector.bn_aggr(mean_var[:, t % 2, :], stats[:]).then_inc(aggr_done, 1)

            def normalise(b, t):
                if have(b):
                    dve.wait_ge(rstd_done, due(4 * b + t + 1))
                    nc.vector.tensor_scalar(x_tile[:, t % 2, :], x_tile[:, t % 2, :], mean_var[:, t % 2, 0:1],
                                            rstd[:, t % 2, :], ALU.subtract, ALU.mult).then_inc(norm_done, 1)

            def form_bias(b, t):
                if have(b):
                    dve.wait_ge(m_turned, due(2 * b))
                    dve.wait_ge(masked_max, due(64 * (b - 1) + 48 + 4 * t + 4))
                    dve.wait_ge(adj_in, due(16 * (4 * b + t + 1)) if known(b) else next_adj.reg)
                    if not known(b):
                        next_adj.advance()
                    nc.vector.tensor_scalar(bias_q[:, t, :], adj_tile[:], 0.0, MASKED, ALU.is_equal, ALU.mult
                                            ).then_inc(bias_done, 1)

            def form_c(b, g):
                dve.wait_ge(ln_done, due(4 * b + g + 1))
                nc.vector.tensor_tensor(c_all[:], neg_max[:, g % 2, :], ln_sum[:], ALU.subtract).then_inc(c_sum_done, 1)
                dve.wait_ge(c_sum_done, due(4 * b + g + 1))
                dve.wait_ge(c_turned, due(4 * b + g))
                nc.vector.tensor_scalar(c_parts[:, 0, :], c_all[:], 1.0 / SCALE, None, ALU.mult).then_inc(c_hi_done, 1)
                dve.wait_ge(c_hi_done, due(4 * b + g + 1))
                nc.vector.scalar_tensor_tensor(out=c_parts[:, 1, :], in0=c_all[:], scalar=1.0 / SCALE,
                                               in1=c_parts[:, 0, :].bitcast(F32), op0=ALU.mult, op1=ALU.subtract
                                               ).then_inc(c_lo_done, 1)

            def take_turn(k, kind, n, rel):
                b = k + rel
                if not have(b):
                    return
                if kind == "h":
                    dve.wait_ge(h_hi_done, due(4 * b + n + 1))
                    nc.vector.scalar_tensor_tensor(
                        out=hT_lo[:, :, P * n:P * n + P], in0=bank1((kind, n, rel)).rearrange("p (t q) -> p t q", q=P), scalar=0.0,
                        in1=hT_hi[:, :, P * n:P * n + P].bitcast(F32), op0=ALU.max, op1=ALU.subtract
                    ).then_inc(h_lo_done, 1)
                elif kind == "m":
                    dve.wait_ge(m_turned, due(2 * b + n + 1))
                    dve.wait_ge(scores2, due(64 * (b - 1) + 48 + 8 * n + 8))
                    dve.wait_ge(probs_masked, due(MASKED_ALL * (b - 1) + masked_before(48 + 8 * n + 8)))
                    nc.vector.tensor_copy(bias_k[:, 2 * n:2 * n + 2, :], bank1((kind, n, rel)).bitcast(BF16).rearrange("p (t q) -> p t q", q=S)
                                          ).then_inc(m_done, 1)
                else:
                    dve.wait_ge(c_turned, due(4 * b + n + 1))
                    dve.wait_ge(c_in, due(32 * (4 * b + n)))
                    nc.vector.tensor_copy(c_rows[:], bank1((kind, n, rel))[0:32, 0:P]).then_inc(c_rows_done, 1)

            def split_weight(n):
                w = "qkvo"[n]
                dve.wait_ge(w_hi_done, n + 1)
                nc.vector.tensor_tensor(w_lo[w][:], probs[:, 4 * (n % 2):4 * (n % 2) + 4, :], w_hi[w][:].bitcast(F32),
                                        ALU.subtract).then_inc(w_lo_done, 1)

            def step(k, parity):
                for u in range(SLOTS):
                    if known(k) and k == 0:
                        if u in SPLIT_AT:
                            split_weight(SPLIT_AT.index(u))
                        if u == 16:
                            dve.wait_ge(small_in, 64)
                    for kind, n, rel in TURNS.get(u, ()):
                        if kind == "c":
                            take_turn(k, kind, n, rel)
                    b, n = pass1(k, u)
                    if have(b):
                        g, qt, j = n // 16, n % 16 // 4, n % 4
                        col = 4 * j + qt
                        if g == 0 and j == 0:
                            dve.wait_ge(bias_done, due(4 * b + qt + 1))
                        dve.wait_ge(scores1, due(64 * b + n + 1) if known(b) else next_scores.reg)
                        if not known(b):
                            next_scores.advance()
                        nc.vector.tensor_tensor_reduce(bank1(("s", u)), bank1(("s", u)), bias_q[:, qt, :], -SCALE, 3.0e38,
                                                       ALU.add, ALU.min, neg_max[:, g % 2, col:col + 1]
                                                       ).then_inc(masked_max, 1)
                    b, n = pass2(k, u - 1) if u else pass2(k - 1, SLOTS - 1)
                    if have(b) and n % 8 in VECTOR_MASKED:
                        dve.wait_ge(exp2_done, due(64 * b + n + 1))
                        nc.vector.scalar_tensor_tensor(out=probs[:, n % P_RING, :], in0=bias_k[:, n % 16 // 4, :], scalar=-MASKED,
                                                       in1=probs[:, n % P_RING, :], op0=ALU.add, op1=ALU.min
                                                       ).then_inc(probs_masked, 1)
                    if u in C_AT:
                        g, rel = C_AT[u]
                        if have(k + rel):
                            form_c(k + rel, g)
                    for kind, n, rel in TURNS.get(u - 1, ()):
                        if kind != "c":
                            take_turn(k, kind, n, rel)
                    if u in O_LO_AT and have(k - 1):
                        g = O_LO_AT[u]
                        dve.wait_ge(o_hi_done, due(4 * (k - 1) + g + 1))
                        nc.vector.scalar_tensor_tensor(out=oT_lo[:, g, :], in0=psO[:], scalar=bv_col[:, g:g + 1],
                                                       in1=oT_hi[:, g, :].bitcast(F32), op0=ALU.add, op1=ALU.subtract
                                                ).then_inc(o_lo_done, 1)
                    if u % 4 == 1:
                        T, kb = (u // 4 - 1, k) if u >= 4 else (15, k - 1)
                        kind, n = TILES[T]
                        b = kb - 2 if kind == "o" else kb
                        if have(b) and kind == "o":
                            dve.wait_ge(out_done, due(4 * b + n + 1))
                            dve.wait_ge(y_plus_bo, due(4 * b + n + 1))
                            nc.vector.tensor_tensor(y_tile[:, n % 2, :], psP[:, T % 2, :], y_tile[:, n % 2, :], ALU.add
                                                    ).then_inc(y_done, 1)
                        elif have(b) and kind == "v":
                            dve.wait_ge(qkv_done, due(12 * b + QKV_TILES.index((kind, n)) + 1))
                            dve.wait_ge(pv_done, due(16 * (b - 1)))
                            nc.vector.tensor_copy(v_sb[:, parity, n, :], psP[:, T % 2, :]).then_inc(v_done, 1)
                        elif have(b):
                            i = QK_ORDER.index((kind, n))
                            dve.wait_ge(qk_hi_done, due(8 * b + i + 1))
                            bias = (bq_col if kind == "q" else bk_col)[:, n:n + 1]
                            wait_stack_loaded(*((b, i - 2) if i >= 2 else (b - 1, i + 6)))
                            nc.vector.scalar_tensor_tensor(out=part_lo[:, i % 2, :], in0=psP[:, T % 2, :], scalar=bias,
                                                           in1=part_hi[:, i % 2, :].bitcast(F32), op0=ALU.add, op1=ALU.subtract
                                                           ).then_inc(qk_lo_done, 1)
                    if u in BIAS_AT: form_bias(k, BIAS_AT.index(u))
                    if u == 4: ln_stats(k, 2)
                    if u == 7: normalise(k, 2)
                    if u == 9: ln_stats(k, 3)
                    if u == 12: normalise(k, 3)
                    if u == 40: ln_stats(k + 1, 0)
                    if u == 42: ln_stats(k + 1, 1)
                    if u == 46: normalise(k + 1, 0)
                    if u == 50: normalise(k + 1, 1)

            blocks(dve, step, counters=[(next_scores, 64 * (LOOP_FROM - 1) + SLOTS - S1_AT + 1),
                                        (next_stats, 4 * LOOP_FROM + 3), (next_adj, 16 * (4 * LOOP_FROM + 1))])

        @block.tensor
        def _(pe):
            def wait_tile_out(k, T):
                kind, n = TILES[T]
                if not have(k - 2 if kind == "o" else k):
                    return
                if kind == "o":
                    pe.wait_ge(y_done, due(4 * (k - 2) + n + 1))
                elif kind == "v":
                    pe.wait_ge(v_done, due(4 * k + n + 1))
                else:
                    i = QK_ORDER.index((kind, n))
                    pe.wait_ge(qk_hi_done, due(8 * k + i + 1))
                    pe.wait_ge(qk_lo_done, due(8 * k + i + 1))

            def wait_bank1(k, item):
                at = RING.index(item)
                before = [(k, i) for i in reversed(range(at))] + [(k - 1, i) for i in reversed(range(at, len(RING)))]
                for kb, i in before:
                    if i % 3 != at % 3:
                        continue
                    if RING[i][0] == "s":
                        b, n = pass1(kb, RING[i][1])
                        if have(b):
                            pe.wait_ge(exp1_done, due(64 * b + n + 1))
                            return
                        continue
                    kind, n, rel = RING[i]
                    b = kb + rel
                    if not have(b):
                        continue
                    if kind == "h":
                        pe.wait_ge(h_hi_done, due(4 * b + n + 1))
                        pe.wait_ge(h_lo_done, due(4 * b + n + 1))
                    elif kind == "m":
                        pe.wait_ge(m_done, due(2 * b + n + 1))
                    else:
                        pe.wait_ge(c_rows_done, due(4 * b + n + 1))
                    return

            def three_products(acc, w_h, w_l, m_h, m_l, kt):
                nc.tensor.matmul(acc, w_h, m_h, start=(kt == 0), stop=False)
                nc.tensor.matmul(acc, w_h, m_l, start=False, stop=False)
                return nc.tensor.matmul(acc, w_l, m_h, start=False, stop=(kt == NT - 1))

            def project(k, u):
                T, kt = u // 4, u % 4
                kind, n = TILES[T]
                b = k - 2 if kind == "o" else k
                if not have(b):
                    return
                if kt == 0:
                    wait_tile_out(*((k, T - 2) if T >= 2 else (k - 1, T + 14)))
                    if T == 0:
                        pe.wait_ge(o_hi_done, due(4 * b + 4))
                        pe.wait_ge(o_lo_done, due(4 * b + 4))
                    if T == 4:
                        pe.wait_ge(h_hi_done, due(4 * b + 4))
                        pe.wait_ge(h_lo_done, due(4 * b + 4))
                    if known(k) and k == 0 and n == 0:
                        pe.wait_ge(w_lo_done, "qkv".index(kind) + 1)
                    if known(k) and k == 1 and T == 4:
                        pe.wait_ge(w_lo_done, 4)
                acc = psP[:, T % 2, :]
                rows = slice(P * n, P * n + P)
                if kind in "qk":
                    last = three_products(acc, w_hi[kind][:, kt, rows], w_lo[kind][:, kt, rows],
                                          hT_hi[:, kt, :], hT_lo[:, kt, :], kt)
                elif kind == "v":
                    last = three_products(acc, hT_hi[:, kt, rows], hT_lo[:, kt, rows],
                                          w_hi["v"][:, kt, :], w_lo["v"][:, kt, :], kt)
                else:
                    last = three_products(acc, oT_hi[:, kt, rows], oT_lo[:, kt, rows],
                                          w_hi["o"][:, kt, :], w_lo["o"][:, kt, :], kt)
                if kt == NT - 1:
                    last.then_inc(out_done if kind == "o" else qkv_done, 1)

            def turn(k, kind, n, rel):
                b = k + rel
                if not have(b):
                    return
                bank = bank1((kind, n, rel))
                wait_bank1(k, (kind, n, rel))
                if kind == "h":
                    pe.wait_ge(norm_done, due(4 * b + n + 1))
                    for t in range(NT):
                        last = nc.tensor.transpose(bank[:, P * t:P * t + P], x_tile[:, n % 2, P * t:P * t + P], ident[:])
                    last.then_inc(h_turned, 1)
                elif kind == "m":
                    pe.wait_ge(bias_done, due(4 * b + 4))
                    for i in range(2 * NT):
                        key_tile, t = 2 * n + i // NT, i % NT
                        last = nc.tensor.transpose(bank[:, 64 * i:64 * i + 64].bitcast(BF16),
                                                   bias_q[:, t, P * key_tile:P * key_tile + P], ident_b[:])
                    last.then_inc(m_turned, 1)
                else:
                    pe.wait_ge(c_lo_done, due(4 * b + n + 1))
                    nc.tensor.transpose(bank[0:32, 0:P], c_parts[:].rearrange("p a n -> p (a n)").bitcast(F32), ident[:]
                                        ).then_inc(c_turned, 1)

            def step(k, parity):
                for u in range(SLOTS):
                    for kind, n, rel in TURNS.get(u, ()):
                        if kind == "c":
                            turn(k, kind, n, rel)
                    b, n = pass1(k, u)
                    if have(b):
                        g, qt, j = n // 16, n % 16 // 4, n % 4
                        if n % 16 == 0:
                            pe.wait_ge(stack_in["q"], due(192 * (4 * b + g + 1)))
                            pe.wait_ge(stack_in["k"], due(192 * (4 * b + g + 1)))
                        wait_bank1(k, ("s", u))
                        nc.tensor.matmul(bank1(("s", u)), q_stack[0:STACK, g, j, P * qt:P * qt + P],
                                         k_stack[0:STACK, g, j, :], start=True, stop=True).then_inc(scores1, 1)
                    b, n = pass2(k, u)
                    if have(b):
                        g, kt, j = n // 16, n % 16 // 4, n % 4
                        if n % 16 == 0:
                            pe.wait_ge(c_in, due(32 * (4 * b + g + 1)))
                        if g == 0 and j == 0:
                            pe.wait_ge(m_done, due(2 * b + kt // 2 + 1))
                        pe.wait_ge(exp2_done, due(64 * b + n - 1))
                        last = nc.tensor.matmul(ps2[:, n % 2, :], k_stack[:, g, j, P * kt:P * kt + P], q_stack[:, g, j, :],
                                                start=True, stop=(n % 8 in VECTOR_MASKED))
                        if n % 8 not in VECTOR_MASKED:
                            last = nc.tensor.matmul(ps2[:, n % 2, :], ident_b[:], bias_k[:, kt, :], start=False, stop=True)
                        last.then_inc(scores2, 1)
                    project(k, u)
                    if u % 4 == 2 and have(k - 1):
                        b, n = k - 1, u // 4
                        g, kt = n // 4, n % 4
                        if kt == 0:
                            pe.wait_ge(o_hi_done, due(4 * b + g))
                            pe.wait_ge(o_lo_done, due(4 * b + g))
                        if g == 0:
                            pe.wait_ge(v_done, due(4 * b + kt + 1))
                        pe.wait_ge(exp2_done, due(64 * b + 4 * n + 4))
                        pe.wait_ge(probs_masked, due(MASKED_ALL * b + masked_before(4 * n + 4)))
                        for j in range(GROUP):
                            at = DH * (GROUP * g + j)
                            last = nc.tensor.matmul(psO[32 * j:32 * j + 32, :], v_sb[:, 1 - parity, kt, at:at + DH],
                                                    probs[:, (4 * n + j) % P_RING, :], start=(kt == 0), stop=(kt == NT - 1))
                        last.then_inc(pv_done, 1)
                    for kind, n, rel in TURNS.get(u, ()):
                        if kind != "c":
                            turn(k, kind, n, rel)

            pe.wait_ge(ident_done, 4)
            blocks(pe, step)


_INS = ['x', 'adj', 'L0_gnn_Wq', 'L0_gnn_bq', 'L0_gnn_Wk', 'L0_gnn_bk', 'L0_gnn_Wv', 'L0_gnn_bv', 'L0_gnn_Wo', 'L0_gnn_bo']


def kernel(**inputs):
    import numpy as _np
    import concourse.bacc as _bacc
    from concourse import mybir as _mybir
    from concourse.bass_utils import run_bass_kernel_spmd as _run

    nc = _bacc.Bacc("TRN2", target_bir_lowering=False, num_devices=1, dynamic_dma_scratch_size=256)
    arrays, args = {}, []
    for name in _INS:
        a = _np.ascontiguousarray(inputs[name])
        arrays[f"in_{name}_dram"] = a
        args.append(nc.dram_tensor(f"in_{name}_dram", a.shape, _mybir.dt.from_np(a.dtype), kind="ExternalInput").ap())
    out = nc.dram_tensor("out_0_dram", inputs["x"].shape, _mybir.dt.float32, kind="ExternalOutput").ap()
    attention_block(nc, *args, out)
    r = _run(nc, [arrays], core_ids=[0])
    return r.results[0]["out_0_dram"]
```
